# Optimizing a Trainium2 kernel written in Bass

```python
import numpy as np
import jax
import jax.numpy as jnp

def _softmax(x, axis=-1):
    return jax.nn.softmax(x, axis=axis)

def _gelu(x):
    return jax.nn.gelu(x, approximate=True)

def _silu(x):
    return jax.nn.silu(x)

def _sigmoid(x):
    return jax.nn.sigmoid(x)

def _layernorm(x, axis=-1, eps=1e-05):
    m = jnp.mean(x, axis=axis, keepdims=True)
    v = jnp.var(x, axis=axis, keepdims=True)
    return (x - m) / jnp.sqrt(v + eps)

def _scatter_add(tgt, idx, src, axis=0):
    return tgt.at[idx].add(src)

def _segment_sum(src, seg, n):
    return jax.ops.segment_sum(src, seg, n)
kernel_name = 'mk_dlrm_tower_d1_rec_r8_24401c'

def setup_inputs(seed: int=0):
    np.random.seed(seed)
    _w = jnp.asarray

    def _rec_inputs():
        import jax
        import jax.numpy as jnp
        _tk = jax.random.key(seed)
        dense_ctx = jax.random.normal(jax.random.fold_in(_tk, 190), (2048, 16), jnp.float32)
        ids = jnp.stack([jax.random.randint(jax.random.fold_in(_tk, 200 + f), (2048,), 0, v, jnp.int32) for f, v in enumerate([1250, 1000, 1250, 1250, 1250, 1250, 125000, 12500, 1000, 1250, 12500, 1250, 1000, 1250, 12500, 12500, 12500, 1000, 1000, 1250, 1000, 1250, 1000, 1250, 1000, 1250, 1250])], axis=1)
        tbl_0 = 0.05 * jax.random.normal(jax.random.fold_in(_tk, 500 + 0), (1250, 128), jnp.float32)
        tbl_1 = 0.05 * jax.random.normal(jax.random.fold_in(_tk, 500 + 1), (1000, 128), jnp.float32)
        tbl_2 = 0.05 * jax.random.normal(jax.random.fold_in(_tk, 500 + 2), (1250, 128), jnp.float32)
        tbl_3 = 0.05 * jax.random.normal(jax.random.fold_in(_tk, 500 + 3), (1250, 128), jnp.float32)
        tbl_4 = 0.05 * jax.random.normal(jax.random.fold_in(_tk, 500 + 4), (1250, 128), jnp.float32)
        tbl_5 = 0.05 * jax.random.normal(jax.random.fold_in(_tk, 500 + 5), (1250, 128), jnp.float32)
        tbl_6 = 0.05 * jax.random.normal(jax.random.fold_in(_tk, 500 + 6), (125000, 128), jnp.float32)
        tbl_7 = 0.05 * jax.random.normal(jax.random.fold_in(_tk, 500 + 7), (12500, 128), jnp.float32)
        tbl_8 = 0.05 * jax.random.normal(jax.random.fold_in(_tk, 500 + 8), (1000, 128), jnp.float32)
        tbl_9 = 0.05 * jax.random.normal(jax.random.fold_in(_tk, 500 + 9), (1250, 128), jnp.float32)
        tbl_10 = 0.05 * jax.random.normal(jax.random.fold_in(_tk, 500 + 10), (12500, 128), jnp.float32)
        tbl_11 = 0.05 * jax.random.normal(jax.random.fold_in(_tk, 500 + 11), (1250, 128), jnp.float32)
        tbl_12 = 0.05 * jax.random.normal(jax.random.fold_in(_tk, 500 + 12), (1000, 128), jnp.float32)
        tbl_13 = 0.05 * jax.random.normal(jax.random.fold_in(_tk, 500 + 13), (1250, 128), jnp.float32)
        tbl_14 = 0.05 * jax.random.normal(jax.random.fold_in(_tk, 500 + 14), (12500, 128), jnp.float32)
        tbl_15 = 0.05 * jax.random.normal(jax.random.fold_in(_tk, 500 + 15), (12500, 128), jnp.float32)
        tbl_16 = 0.05 * jax.random.normal(jax.random.fold_in(_tk, 500 + 16), (12500, 128), jnp.float32)
        tbl_17 = 0.05 * jax.random.normal(jax.random.fold_in(_tk, 500 + 17), (1000, 128), jnp.float32)
        tbl_18 = 0.05 * jax.random.normal(jax.random.fold_in(_tk, 500 + 18), (1000, 128), jnp.float32)
        tbl_19 = 0.05 * jax.random.normal(jax.random.fold_in(_tk, 500 + 19), (1250, 128), jnp.float32)
        tbl_20 = 0.05 * jax.random.normal(jax.random.fold_in(_tk, 500 + 20), (1000, 128), jnp.float32)
        tbl_21 = 0.05 * jax.random.normal(jax.random.fold_in(_tk, 500 + 21), (1250, 128), jnp.float32)
        tbl_22 = 0.05 * jax.random.normal(jax.random.fold_in(_tk, 500 + 22), (1000, 128), jnp.float32)
        tbl_23 = 0.05 * jax.random.normal(jax.random.fold_in(_tk, 500 + 23), (1250, 128), jnp.float32)
        tbl_24 = 0.05 * jax.random.normal(jax.random.fold_in(_tk, 500 + 24), (1000, 128), jnp.float32)
        tbl_25 = 0.05 * jax.random.normal(jax.random.fold_in(_tk, 500 + 25), (1250, 128), jnp.float32)
        tbl_26 = 0.05 * jax.random.normal(jax.random.fold_in(_tk, 500 + 26), (1250, 128), jnp.float32)
        _rk = jax.random.fold_in(_tk, 7)
        W_top1 = 0.0521996 * jax.random.normal(jax.random.fold_in(_tk, 801), (367, 512), jnp.float32)
        W_top2 = 0.0441942 * jax.random.normal(jax.random.fold_in(_tk, 802), (512, 256), jnp.float32)
        W_top3 = 0.0625 * jax.random.normal(jax.random.fold_in(_tk, 803), (256, 1), jnp.float32)
        b_top1 = jnp.zeros((512,), jnp.float32)
        b_top2 = jnp.zeros((256,), jnp.float32)
        return (dense_ctx, ids, tbl_0, tbl_1, tbl_2, tbl_3, tbl_4, tbl_5, tbl_6, tbl_7, tbl_8, tbl_9, tbl_10, tbl_11, tbl_12, tbl_13, tbl_14, tbl_15, tbl_16, tbl_17, tbl_18, tbl_19, tbl_20, tbl_21, tbl_22, tbl_23, tbl_24, tbl_25, tbl_26, W_top1, b_top1, W_top2, b_top2, W_top3)
    dense_ctx, ids, tbl_0, tbl_1, tbl_2, tbl_3, tbl_4, tbl_5, tbl_6, tbl_7, tbl_8, tbl_9, tbl_10, tbl_11, tbl_12, tbl_13, tbl_14, tbl_15, tbl_16, tbl_17, tbl_18, tbl_19, tbl_20, tbl_21, tbl_22, tbl_23, tbl_24, tbl_25, tbl_26, W_top1, b_top1, W_top2, b_top2, W_top3 = _rec_inputs()

    def _L0_rec_setup():
        import jax, jax.numpy as jnp
        import numpy as np
        NUM_FEATURES = 27
        EMBED_DIM = 128
        BATCH = 4096
        key = jax.random.key(seed)
        inputs = jax.random.normal(key, (BATCH, NUM_FEATURES, EMBED_DIM), dtype=jnp.float32)
        return {'inputs': inputs}
    _L0_rec_all = _L0_rec_setup()
    _L0_rec_in = {k: v for k, v in _L0_rec_all.items() if k in ()}
    del _L0_rec_all
    return {'dense_ctx': dense_ctx, 'ids': ids, 'tbl_0': tbl_0, 'tbl_1': tbl_1, 'tbl_2': tbl_2, 'tbl_3': tbl_3, 'tbl_4': tbl_4, 'tbl_5': tbl_5, 'tbl_6': tbl_6, 'tbl_7': tbl_7, 'tbl_8': tbl_8, 'tbl_9': tbl_9, 'tbl_10': tbl_10, 'tbl_11': tbl_11, 'tbl_12': tbl_12, 'tbl_13': tbl_13, 'tbl_14': tbl_14, 'tbl_15': tbl_15, 'tbl_16': tbl_16, 'tbl_17': tbl_17, 'tbl_18': tbl_18, 'tbl_19': tbl_19, 'tbl_20': tbl_20, 'tbl_21': tbl_21, 'tbl_22': tbl_22, 'tbl_23': tbl_23, 'tbl_24': tbl_24, 'tbl_25': tbl_25, 'tbl_26': tbl_26, 'W_top1': W_top1, 'b_top1': b_top1, 'W_top2': W_top2, 'b_top2': b_top2, 'W_top3': W_top3}

def reference(dense_ctx, ids, tbl_0, tbl_1, tbl_2, tbl_3, tbl_4, tbl_5, tbl_6, tbl_7, tbl_8, tbl_9, tbl_10, tbl_11, tbl_12, tbl_13, tbl_14, tbl_15, tbl_16, tbl_17, tbl_18, tbl_19, tbl_20, tbl_21, tbl_22, tbl_23, tbl_24, tbl_25, tbl_26, W_top1, b_top1, W_top2, b_top2, W_top3):
    import jax
    import jax.numpy as jnp

    def _L0_rec_ref(inputs):
        import jax, jax.numpy as jnp
        import numpy as np
        NUM_FEATURES = 27
        EMBED_DIM = 128
        BATCH = 4096
        interactions = jnp.einsum('bnd,bmd->bnm', inputs, inputs)
        n = inputs.shape[1]
        i, j = jnp.triu_indices(n, k=1)
        return interactions[:, i, j]
    e = jnp.stack([tbl_0[ids[:, 0]], tbl_1[ids[:, 1]], tbl_2[ids[:, 2]], tbl_3[ids[:, 3]], tbl_4[ids[:, 4]], tbl_5[ids[:, 5]], tbl_6[ids[:, 6]], tbl_7[ids[:, 7]], tbl_8[ids[:, 8]], tbl_9[ids[:, 9]], tbl_10[ids[:, 10]], tbl_11[ids[:, 11]], tbl_12[ids[:, 12]], tbl_13[ids[:, 13]], tbl_14[ids[:, 14]], tbl_15[ids[:, 15]], tbl_16[ids[:, 16]], tbl_17[ids[:, 17]], tbl_18[ids[:, 18]], tbl_19[ids[:, 19]], tbl_20[ids[:, 20]], tbl_21[ids[:, 21]], tbl_22[ids[:, 22]], tbl_23[ids[:, 23]], tbl_24[ids[:, 24]], tbl_25[ids[:, 25]], tbl_26[ids[:, 26]]], axis=1)
    z = _L0_rec_ref(e)
    z = z.reshape(z.shape[0], -1)
    h = jnp.concatenate([z, dense_ctx], axis=1)
    h = jnp.maximum(h @ W_top1 + b_top1, 0.0)
    h = jnp.maximum(h @ W_top2 + b_top2, 0.0)
    y = h @ W_top3
    return y

_drawn_inputs = setup_inputs


def setup_inputs(seed=0):
    import zlib

    import numpy as np

    out = dict(_drawn_inputs(seed))
    spreads = {'b_top1': (0.0, 0.1), 'b_top2': (0.0, 0.1)}
    factors = {}
    for name, (base, spread) in spreads.items():
        noise = np.random.default_rng([zlib.crc32(name.encode()), seed]).standard_normal(out[name].shape)
        drawn = base * np.exp(spread * noise) if base else spread * noise
        out[name] = jnp.asarray(drawn.astype(out[name].dtype))
    for name, factor in factors.items():
        out[name] = (out[name] * factor).astype(out[name].dtype)
    return out
```

```python
from contextlib import ExitStack

import numpy as np

import concourse.bass as bass
from concourse import mybir

P = 128
FEATURES = 27
DIM = 128
BATCH = 2048
CTX = 16
HID1, HID2 = 512, 256
TILES = BATCH // P
GROUP = 4
GROUPS = TILES // GROUP
WIDE = GROUP * P
QUAD = 32
QUADS = P // QUAD
SLOT = 7
TURNS = (FEATURES + 3) // 4
UNIT_SETS = 8
UNIT = UNIT_SETS * QUADS
UNITS = P // UNIT
TURNS_PER_BANK = GROUP * TURNS // 2
WEIGHT_LOADS = 5


def turn_slots(k):
    return min(4, FEATURES - 4 * k)


def tower(nc, ids, tables, ctx_rows, w1, b1, w2, b2, w3, out):
    fp32 = mybir.dt.float32
    ACT = mybir.ActivationFunctionType
    ALU = mybir.AluOpType
    with ExitStack() as stack:
        def sb(name, shape, dt=fp32):
            return stack.enter_context(nc.sbuf_tensor(name, shape, dt))

        def sem(name):
            return stack.enter_context(nc.semaphore(name))

        ids_sb = sb("ids_sb", [P, TILES * FEATURES], mybir.dt.int32)
        ids_now = sb("ids_now", [P, GROUP * FEATURES], mybir.dt.int32)
        rows = sb("rows", [P, GROUP, FEATURES, DIM])
        emb = sb("emb", [P, 2, P, QUAD])
        inter = sb("inter", [P, SLOT, WIDE])
        hid1 = sb("hid1", [P, HID1 // P, WIDE])
        hid2 = sb("hid2", [P, HID2 // P, WIDE])
        w1_sb = sb("w1_sb", [P, SLOT, HID1])
        w2_sb = sb("w2_sb", [P, HID1 // P, HID2])
        w3_sb = sb("w3_sb", [P, HID2 // P])
        b1_sb = sb("b1_sb", [P, HID1 // P])
        b2_sb = sb("b2_sb", [P, HID2 // P])
        ctx_sb = sb("ctx_sb", [P, TILES, CTX])
        ctx_t = sb("ctx_t", [P, BATCH])
        ident = sb("ident", [P, P])
        y_sb = sb("y_sb", [P, TILES])

        ps_t = [stack.enter_context(nc.psum_tensor(f"ps_t{i}", [P, 4, P], fp32)) for i in range(2)]
        ps_g = [stack.enter_context(nc.psum_tensor(f"ps_g{i}", [P, UNIT_SETS, P], fp32)) for i in range(2)]
        ps_h = [stack.enter_context(nc.psum_tensor(f"ps_h{i}", [P, WIDE], fp32)) for i in range(2)]

        ids_in = sem("ids_in")
        ids_staged = sem("ids_staged")
        pool_passed = sem("pool_passed")
        ctx_in = sem("ctx_in")
        weights_in = sem("weights_in")
        ident_zero = sem("ident_zero")
        ident_ready = sem("ident_ready")
        rows_in = [[sem(f"rows_in_{s}_{k}") for k in range(TURNS)] for s in range(GROUP)]
        turn_done = [sem(f"turn_done_{i}") for i in range(2)]
        turn_out = [sem(f"turn_out_{i}") for i in range(2)]
        pads_zero = sem("pads_zero")
        unit_done = [sem(f"unit_done_{i}") for i in range(2)]
        unit_out_dve = sem("unit_out_dve")
        unit_out_act = sem("unit_out_act")
        ctx_turned = sem("ctx_turned")
        ctx_t_ready = sem("ctx_t_ready")
        ctx_placed = sem("ctx_placed")
        layer1_done = sem("layer1_done")
        layer1_out = sem("layer1_out")
        layer2_done = sem("layer2_done")
        layer2_out = sem("layer2_out")
        layer3_done = sem("layer3_done")
        layer3_out = sem("layer3_out")
        out_stored = sem("out_stored")

        block = stack.enter_context(nc.Block())

        @block.sync
        def _(sp):
            sp.dma_start(ids_sb[:, :], ids).then_inc(ids_in, 16)
            sp.dma_start(ctx_sb[:, :, :], ctx_rows).then_inc(ctx_in, 16)
            sp.dma_start(w1_sb[:, :, :], w1).then_inc(weights_in, 16)
            sp.dma_start(w2_sb[:, :, :], w2).then_inc(weights_in, 16)
            sp.dma_start(b1_sb[:, :], b1).then_inc(weights_in, 16)
            sp.dma_start(b2_sb[:, :], b2).then_inc(weights_in, 16)
            sp.dma_start(w3_sb[:, :], w3).then_inc(weights_in, 16)
            sp.wait_ge(layer3_out, GROUPS + 1)
            sp.dma_start(out, y_sb[:, :]).then_inc(out_stored, 16)
            sp.wait_ge(out_stored, 16)

        @block.gpsimd
        def _(pool):
            nc.gpsimd.memset(ident[:, :], 0.0).then_inc(ident_zero, 1)
            pool.wait_ge(ident_zero, 1)
            nc.gpsimd.affine_select(out=ident[:, :], in_=ident[:, :], compare_op=ALU.not_equal, fill=1.0,
                                    base=0, pattern=[[-1, P]], channel_multiplier=1).then_inc(ident_ready, 1)
            pool.wait_ge(ids_in, 16)

            def gather_group(indices, g):
                for s in range(GROUP):
                    if g is not None:
                        last = (s + 1) * TURNS - 1
                        pool.wait_ge(turn_done[last % 2], (g - 1) * TURNS_PER_BANK + (last // 2 + 1))
                        pool.sem_inc(pool_passed, 1)
                    for f in range(FEATURES):
                        at = s * FEATURES + f
                        nc.gpsimd.indirect_dma_start(
                            rows[:, s, f, :], None, tables[f],
                            bass.IndirectOffsetOnAxis(ap=indices[:, at:at + 1], axis=0),
                        ).then_inc(rows_in[s][f // 4], 16)

            gather_group(ids_sb, None)
            with pool.Fori(1, GROUPS) as g:
                last = GROUP * TURNS - 1
                pool.wait_ge(turn_done[last % 2], g * TURNS_PER_BANK)
                pool.sem_inc(pool_passed, 1)
                nc.gpsimd.tensor_copy(ids_now[:, :], ids_sb[:, bass.ds(g * (GROUP * FEATURES), GROUP * FEATURES)]
                                      ).then_inc(ids_staged, 1)
                pool.wait_ge(ids_staged, g)
                pool.sem_inc(pool_passed, 1)
                gather_group(ids_now, g)

        @block.tensor
        def _(pe):
            pe.wait_ge(ident_ready, 1)
            pe.wait_ge(ctx_in, 16)
            for t in range(TILES):
                last = nc.tensor.transpose(ps_g[t // UNIT_SETS][0:CTX, t % UNIT_SETS, :], ctx_sb[:, t, :], ident[:, :])
            last.then_inc(ctx_turned, 1)
            pe.wait_ge(ctx_t_ready, 2)
            pe.wait_ge(pads_zero, 2)
            pe.wait_ge(weights_in, 16 * WEIGHT_LOADS)
            with pe.Fori(0, GROUPS) as g:
                for s in range(GROUP):
                    for k in range(TURNS):
                        turn = s * TURNS + k
                        pe.wait_ge(rows_in[s][k], (g + 1) * (16 * turn_slots(k)))
                        pe.wait_ge(turn_out[turn % 2], g * TURNS_PER_BANK + (turn // 2 + 1))
                        for i in range(turn_slots(k)):
                            last = nc.tensor.transpose(ps_t[turn % 2][:, i, :], rows[:, s, 4 * k + i, :], ident[:, :])
                        last.then_inc(turn_done[turn % 2], 1)
                    for i in range(2):
                        pe.wait_ge(turn_out[i], g * TURNS_PER_BANK + (((s + 1) * TURNS + 1 - i) // 2 + 1))
                    for u in range(UNITS):
                        unit = s * UNITS + u
                        pe.wait_ge(unit_out_dve, g * (GROUP * UNITS) + (unit + 1))
                        pe.wait_ge(unit_out_act, g * (GROUP * UNITS) + (unit + 1))
                        for c in range(UNIT_SETS):
                            b = u * UNIT + c * QUADS
                            last = nc.tensor.matmul(
                                ps_g[unit % 2][:, c, 0:QUADS * FEATURES].rearrange("p (b f) -> p b f", b=QUADS),
                                emb[:, s % 2, b:b + QUADS, :].rearrange("p b f -> p (b f)"),
                                emb[:, s % 2, b:b + QUADS, 0:FEATURES], start=True, stop=True)
                        last.then_inc(unit_done[unit % 2], 1)
                pe.wait_ge(unit_out_dve, (g + 1) * (GROUP * UNITS) + 2)
                pe.wait_ge(unit_out_act, (g + 1) * (GROUP * UNITS) + 2)
                pe.wait_ge(ctx_placed, g + 1)
                for c in range(HID1 // P):
                    if c < 2:
                        pe.wait_ge(layer3_out, g + 1)
                    else:
                        pe.wait_ge(layer1_out, g * (HID1 // P) + (c - 1))
                    for j in range(SLOT):
                        last = nc.tensor.matmul(ps_h[c % 2][:, :], w1_sb[:, j, c * P:(c + 1) * P], inter[:, j, :],
                                                start=(j == 0), stop=(j == SLOT - 1))
                    last.then_inc(layer1_done, 1)
                pe.wait_ge(layer1_out, (g + 1) * (HID1 // P))
                for c in range(HID2 // P):
                    for j in range(HID1 // P):
                        last = nc.tensor.matmul(ps_h[c % 2][:, :], w2_sb[:, j, c * P:(c + 1) * P], hid1[:, j, :],
                                                start=(j == 0), stop=(j == HID1 // P - 1))
                    last.then_inc(layer2_done, 1)
                pe.wait_ge(layer2_out, (g + 1) * (HID2 // P))
                for s in range(GROUP):
                    for j in range(HID2 // P):
                        last = nc.tensor.matmul(ps_h[0][:, s:s + 1], hid2[:, j, s * P:(s + 1) * P], w3_sb[:, j:j + 1],
                                                start=(j == 0), stop=(j == HID2 // P - 1))
                last.then_inc(layer3_done, 1)

        def copy_turn(engine, copy, s, k, g):
            turn, n = s * TURNS + k, turn_slots(k)
            engine.wait_ge(turn_done[turn % 2], g * TURNS_PER_BANK + (turn // 2 + 1))
            copy(emb[:, s % 2, :, 4 * k:4 * k + n], ps_t[turn % 2][:, 0:n, :].rearrange("p f b -> p b f")
                 ).then_inc(turn_out[turn % 2], 1)

        def copy_blocks(copy, unit, which, done):
            for j in which:
                for q in range(QUADS):
                    n = min(SLOT, FEATURES - q * SLOT)
                    to = inter[QUAD * q:QUAD * (q + 1), 0:n, unit * UNIT:(unit + 1) * UNIT]
                    last = copy(to.rearrange("p m (c b) -> p b c m", b=QUADS)[:, j],
                                ps_g[unit % 2][QUAD * j:QUAD * (j + 1), :,
                                               j * FEATURES + q * SLOT:j * FEATURES + q * SLOT + n])
            last.then_inc(done, 1)

        @block.vector
        def _(dve):
            dve.sem_inc(turn_out[0], 1)
            dve.sem_inc(unit_out_dve, 2)
            dve.sem_inc(layer3_out, 1)
            nc.vector.memset(emb[:, :, :, FEATURES:QUAD], 0.0).then_inc(pads_zero, 1)
            nc.vector.memset(inter[P - QUAD:P, SLOT - 1, :], 0.0).then_inc(pads_zero, 1)
            dve.wait_ge(ctx_turned, 1)
            nc.vector.tensor_copy(ctx_t[P - QUAD:P - QUAD + CTX, 0:BATCH // 2],
                                  ps_g[0][0:CTX, :, :].rearrange("p t b -> p (t b)")).then_inc(ctx_t_ready, 1)
            with dve.Fori(0, GROUPS) as g:
                for s in range(GROUP):
                    for k in range(TURNS):
                        if (s * TURNS + k) % 2 == 0:
                            copy_turn(dve, nc.vector.tensor_copy, s, k, g)
                    for unit in range(s * UNITS, (s + 1) * UNITS):
                        dve.wait_ge(unit_done[unit % 2], g * (GROUP * UNITS // 2) + (unit // 2 + 1))
                        copy_blocks(nc.vector.tensor_copy, unit, (0, 1), unit_out_dve)
                dve.wait_ge(layer3_done, g + 1)
                nc.vector.tensor_copy(y_sb[:, bass.ds(g * GROUP, GROUP)], ps_h[0][:, 0:GROUP]).then_inc(layer3_out, 1)

        @block.scalar
        def _(act):
            act.sem_inc(turn_out[1], 1)
            act.sem_inc(unit_out_act, 2)
            act.wait_ge(ctx_turned, 1)
            nc.scalar.copy(ctx_t[P - QUAD:P - QUAD + CTX, BATCH // 2:BATCH],
                           ps_g[1][0:CTX, :, :].rearrange("p t b -> p (t b)")).then_inc(ctx_t_ready, 1)
            act.wait_ge(ctx_t_ready, 2)
            act.wait_ge(pads_zero, 2)
            act.wait_ge(weights_in, 16 * WEIGHT_LOADS)
            with act.Fori(0, GROUPS) as g:
                for s in range(GROUP):
                    for k in range(TURNS):
                        if (s * TURNS + k) % 2 == 1:
                            copy_turn(act, nc.scalar.copy, s, k, g)
                    if s == 0:
                        nc.scalar.copy(inter[P - QUAD:P - QUAD + CTX, SLOT - 1, :],
                                       ctx_t[P - QUAD:P - QUAD + CTX, bass.ds(g * WIDE, WIDE)]).then_inc(ctx_placed, 1)
                    for unit in range(s * UNITS, (s + 1) * UNITS):
                        act.wait_ge(unit_done[unit % 2], g * (GROUP * UNITS // 2) + (unit // 2 + 1))
                        copy_blocks(nc.scalar.copy, unit, (2, 3), unit_out_act)
                for c in range(HID1 // P):
                    act.wait_ge(layer1_done, g * (HID1 // P) + (c + 1))
                    nc.scalar.activation(hid1[:, c, :], ps_h[c % 2][:, :], ACT.Relu, bias=b1_sb[:, c:c + 1]
                                         ).then_inc(layer1_out, 1)
                for c in range(HID2 // P):
                    act.wait_ge(layer2_done, g * (HID2 // P) + (c + 1))
                    nc.scalar.activation(hid2[:, c, :], ps_h[c % 2][:, :], ACT.Relu, bias=b2_sb[:, c:c + 1]
                                         ).then_inc(layer2_out, 1)


def spread_rows(w_top1):
    spread = np.zeros((P, SLOT, HID1), w_top1.dtype)
    first, second = np.triu_indices(FEATURES, k=1)
    spread[QUAD * (second // SLOT) + first, second % SLOT] = w_top1[:len(first)]
    spread[P - QUAD:P - QUAD + CTX, SLOT - 1] = w_top1[len(first):]
    return spread


def kernel(**inputs):
    import concourse.bacc as bacc
    from concourse.bass_utils import run_bass_kernel_spmd

    nc = bacc.Bacc("TRN2", target_bir_lowering=False, num_devices=1)
    arrays = {}

    def dram(name, a):
        arrays[name] = a = np.ascontiguousarray(a)
        return nc.dram_tensor(name, a.shape, mybir.dt.from_np(a.dtype), kind="ExternalInput").ap()

    x = {name: np.asarray(a) for name, a in inputs.items()}
    out = nc.dram_tensor("y", (BATCH, 1), mybir.dt.float32, kind="ExternalOutput").ap()
    tower(
        nc,
        dram("ids", x["ids"].reshape(P, TILES * FEATURES)),
        [dram(f"tbl_{f}", x[f"tbl_{f}"]) for f in range(FEATURES)],
        dram("dense_ctx", x["dense_ctx"].reshape(P, TILES, CTX)),
        dram("w1", spread_rows(x["W_top1"])),
        dram("b1", x["b_top1"].reshape(HID1 // P, P).T),
        dram("w2", x["W_top2"].reshape(HID1 // P, P, HID2).transpose(1, 0, 2)),
        dram("b2", x["b_top2"].reshape(HID2 // P, P).T),
        dram("w3", x["W_top3"].reshape(HID2 // P, P).T),
        out.rearrange("(p t) o -> p (t o)", p=P),
    )
    results = run_bass_kernel_spmd(nc, [arrays], core_ids=[0]).results[0]
    return results["y"]
```

```python
from contextlib import ExitStack

import numpy as np

import concourse.bass as bass
from concourse import mybir

P = 128
FEATURES = 27
DIM = 128
BATCH = 2048
CTX = 16
HID1, HID2 = 512, 256
TILES = BATCH // P
GROUP = 2
GROUPS = TILES // GROUP
PAIRS = (GROUPS - 2) // 2
WIDE = GROUP * P
QUAD = 32
QUADS = P // QUAD
SLOT = 7
UNIT_SETS = 8
UNIT = UNIT_SETS * QUADS
UNITS = WIDE // UNIT
SMALL_ROWS = 1000
CHUNKS = 8
ROWS_P = SMALL_ROWS // CHUNKS
SMALL = 8
LARGE = FEATURES - SMALL
TURNS = (LARGE + 3) // 4
GROUP_TURNS = SMALL // 2 + GROUP * TURNS
PER_BANK = GROUP_TURNS // 2
CTX_AT = P - QUAD


def turn_slots(k):
    return min(4, LARGE - 4 * k)


ORDER = [("tile", 0, 0)]
for i in range(SMALL // 2):
    ORDER += [("tile", 0, i + 1), ("small", 2 * i)]
ORDER += [("tile", 1, k) for k in range(TURNS)]


def small_turn(k):
    return ORDER.index(("small", k - k % 2))


def tile_turn(s, k):
    return ORDER.index(("tile", s, k))


def tower(nc, ids, ids_small, large_tables, small_tables, ctx_t, w1_upper, w1_lower, b1, w2, b2, w3, out):
    fp32, fp32r, int32 = mybir.dt.float32, mybir.dt.float32r, mybir.dt.int32
    ACT = mybir.ActivationFunctionType
    ALU = mybir.AluOpType
    with ExitStack() as stack:
        def sb(name, shape, dt=fp32):
            return stack.enter_context(nc.sbuf_tensor(name, shape, dt))

        def sem(name):
            return stack.enter_context(nc.semaphore(name))

        ids_sb = sb("ids_sb", [P, TILES * LARGE], int32)
        ids_now = sb("ids_now", [P, GROUP, LARGE], int32)
        rows = sb("rows", [P, GROUP, LARGE, DIM])
        side = sb("side", [P, BATCH])
        ids_row = sb("ids_row", [SMALL, WIDE], fp32r)
        picks = sb("picks", [SMALL, SMALL, P], fp32r)
        row_no = sb("row_no", [P, CHUNKS])
        raw = sb("raw", [P, 2, 2, HID1])
        row_int = sb("row_int", [P, CHUNKS], int32)
        table_h = sb("table_h", [P, SMALL, CHUNKS, DIM], fp32r)
        table_l = sb("table_l", [P, SMALL, CHUNKS, DIM], fp32r)
        onehot = sb("onehot", [P, 2, CHUNKS, WIDE], fp32r)
        emb = sb("emb", [P, WIDE, QUAD])
        inter_h = sb("inter_h", [P, 2, SLOT, WIDE], fp32r)
        inter_l = sb("inter_l", [P, 2, SLOT, WIDE], fp32r)
        hid1 = sb("hid1", [P, HID1 // P, WIDE])
        hid2 = sb("hid2", [P, HID2 // P, WIDE])
        raw_table = emb[:, :, :].rearrange("p b f -> p (b f)").rearrange("p (n c) -> p n c", n=SMALL)
        w2_sb = sb("w2_sb", [P, HID1 // P, HID2])
        raw_w1 = [raw[:, 0], raw[:, 1]] + [
            a[:, :, :].rearrange("p a b -> p (a b)").rearrange("p (h n) -> p h n", h=2) for a in (hid1, w2_sb)]
        low_h = inter_h[:, 1, 0:HID1 // WIDE, :].rearrange("p m b -> p (m b)")
        low_raw = hid2[:, :, :].rearrange("p c b -> p (c b)")
        w1_sb = sb("w1_sb", [P, SLOT, HID1], fp32r)
        w3_sb = sb("w3_sb", [P, HID2 // P])
        b1_sb = sb("b1_sb", [P, HID1 // P])
        b2_sb = sb("b2_sb", [P, HID2 // P])
        ident = sb("ident", [P, P])
        y_sb = sb("y_sb", [P, TILES])

        ps_t = [stack.enter_context(nc.psum_tensor(f"ps_t{i}", [P, 4 * P], fp32)) for i in range(2)]
        ps_g = [stack.enter_context(nc.psum_tensor(f"ps_g{i}", [P, UNIT_SETS, P], fp32)) for i in range(2)]
        ps_h = stack.enter_context(nc.psum_tensor("ps_h", [P, 2, WIDE], fp32))
        ps_i = stack.enter_context(nc.psum_tensor("ps_i", [P, 2, WIDE], fp32))

        ids_in = sem("ids_in")
        ids_staged = sem("ids_staged")
        pool_passed = sem("pool_passed")
        ids_small_in = sem("ids_small_in")
        ctx_in = sem("ctx_in")
        weights_in = sem("weights_in")
        table_in = [sem(f"table_in_{n}") for n in range(SMALL)]
        table_high = sem("table_high")
        table_split = sem("table_split")
        w1_in = [sem(f"w1_in_{j}") for j in range(SLOT)]
        w1_high = sem("w1_high")
        w1_split = sem("w1_split")
        const_zero = sem("const_zero")
        const_made = sem("const_made")
        pads_zero = sem("pads_zero")
        picks_made = sem("picks_made")
        row_no_made = sem("row_no_made")
        low_made = sem("low_made")
        ids_row_ready = sem("ids_row_ready")
        ids_spread = sem("ids_spread")
        onehot_ready = [sem(f"onehot_ready_{i}") for i in range(2)]
        onehot_used = [sem(f"onehot_used_{i}") for i in range(2)]
        rows_in = [[sem(f"rows_in_{s}_{k}") for k in range(TURNS)] for s in range(GROUP)]
        transposed = sem("transposed")
        turn_out = [sem(f"turn_out_{i}") for i in range(2)]
        unit_done = sem("unit_done")
        unit_high = sem("unit_high")
        unit_low = sem("unit_low")
        layer1_done = sem("layer1_done")
        layer1_out = sem("layer1_out")
        layer2_done = sem("layer2_done")
        layer2_out = sem("layer2_out")
        layer3_done = sem("layer3_done")
        layer3_out = sem("layer3_out")
        out_stored = sem("out_stored")

        def block_aps(u, j, q, inter):
            n = min(SLOT, FEATURES - q * SLOT)
            to = inter[QUAD * q:QUAD * (q + 1), 0:n, u * UNIT:(u + 1) * UNIT]
            of = ps_g[u % 2][QUAD * j:QUAD * (j + 1), :, j * FEATURES + q * SLOT:j * FEATURES + q * SLOT + n]
            return to.rearrange("p m (c b) -> p b c m", b=QUADS)[:, j], of

        block = stack.enter_context(nc.Block())

        @block.sync
        def _(sp):
            sp.dma_start(ids_sb[:, :], ids).then_inc(ids_in, 16)
            sp.dma_start(side[0:SMALL, :].bitcast(int32), ids_small).then_inc(ids_small_in, 16)
            for n in range(SMALL):
                sp.dma_start(raw_table[0:ROWS_P, n, :], small_tables[n].rearrange("(p c) d -> p (c d)", c=CHUNKS)
                             ).then_inc(table_in[n], 16)
            sp.wait_ge(picks_made, 1)
            for j in range(SLOT):
                if j >= len(raw_w1):
                    sp.wait_ge(w1_split, j + 1 - len(raw_w1))
                sp.dma_start(raw_w1[j % len(raw_w1)][:, 0, :], w1_upper[:, j, :]).then_inc(w1_in[j], 16)
                sp.dma_start(raw_w1[j % len(raw_w1)][:, 1, :], w1_lower[:, j, :]).then_inc(w1_in[j], 16)
            for copy in range(2):
                sp.dma_start(side[CTX_AT + copy * CTX:CTX_AT + (copy + 1) * CTX, :], ctx_t).then_inc(ctx_in, 16)
            sp.wait_ge(w1_split, SLOT)
            sp.dma_start(w2_sb[:, :, :], w2).then_inc(weights_in, 16)
            sp.dma_start(b1_sb[:, :], b1).then_inc(weights_in, 16)
            sp.dma_start(b2_sb[:, :], b2).then_inc(weights_in, 16)
            sp.dma_start(w3_sb[:, :], w3).then_inc(weights_in, 16)
            sp.wait_ge(layer3_out, GROUPS + 1)
            sp.dma_start(out, y_sb[:, :]).then_inc(out_stored, 16)
            sp.wait_ge(out_stored, 16)

        @block.gpsimd
        def _(pool):
            def gather_tile(indices, s):
                for i in range(LARGE):
                    nc.gpsimd.indirect_dma_start(
                        rows[:, s, i, :], None, large_tables[i],
                        bass.IndirectOffsetOnAxis(ap=indices[:, i:i + 1], axis=0),
                    ).then_inc(rows_in[s][i // 4], 16)

            nc.gpsimd.memset(ident[:, :], 0.0).then_inc(const_zero, 1)
            nc.gpsimd.memset(hid1[0:SMALL, :, :], 0.0).then_inc(const_zero, 1)
            pool.wait_ge(const_zero, 2)
            nc.gpsimd.affine_select(out=ident[:, :], in_=ident[:, :], compare_op=ALU.not_equal, fill=1.0,
                                    base=0, pattern=[[-1, P]], channel_multiplier=1).then_inc(const_made, 1)
            block_of = hid1[0:SMALL, :, :].rearrange("p c d -> p (c d)").rearrange("p (k d) -> p k d", k=SMALL)
            nc.gpsimd.affine_select(out=block_of, in_=block_of, compare_op=ALU.not_equal, fill=1.0,
                                    base=0, pattern=[[-1, SMALL], [0, P]], channel_multiplier=1).then_inc(const_made, 1)
            nc.gpsimd.iota(row_int[:, :], pattern=[[1, CHUNKS]], base=0,
                           channel_multiplier=CHUNKS).then_inc(const_made, 1)
            pool.wait_ge(ids_in, 16)
            for s in range(GROUP):
                gather_tile(ids_sb[:, s * LARGE:(s + 1) * LARGE], s)
            with pool.Fori(1, GROUPS) as g:
                for s in range(GROUP):
                    pool.wait_ge(transposed, (g - 1) * (GROUP * TURNS) + (s + 1) * TURNS)
                    pool.sem_inc(pool_passed, 1)
                    nc.gpsimd.tensor_copy(ids_now[:, s, :], ids_sb[:, bass.ds(g * (GROUP * LARGE) + s * LARGE, LARGE)]
                                          ).then_inc(ids_staged, 1)
                    pool.wait_ge(ids_staged, (g - 1) * GROUP + (s + 1))
                    pool.sem_inc(pool_passed, 1)
                    gather_tile(ids_now[:, s, :], s)

        @block.tensor
        def _(pe):
            def spread_ids(k, g):
                for i in range(2):
                    last = nc.tensor.matmul(ps_i[:, i, :], picks[:, k + i, :], ids_row[:, :], start=True, stop=True)
                last.then_inc(ids_spread, 1)

            def look_up_small(k, g):
                turn = small_turn(k)
                pe.wait_ge(onehot_ready[k % 2], g * (SMALL // 2) + (k // 2 + 1))
                if k % 2 == 1 and k + 1 < SMALL:
                    spread_ids(k + 1, g)
                if k % 2 == 0:
                    pe.wait_ge(turn_out[turn % 2], g * PER_BANK + (turn // 2 + 1))
                to = ps_t[turn % 2][:, (k % 2) * WIDE:(k % 2 + 1) * WIDE]
                for c in range(CHUNKS):
                    for part in (table_h, table_l):
                        last = nc.tensor.matmul(to, part[0:ROWS_P, k, c, :], onehot[0:ROWS_P, k % 2, c, :],
                                                start=(c == 0 and part is table_h),
                                                stop=(c == CHUNKS - 1 and part is table_l))
                last.then_inc(onehot_used[k % 2], 1)

            def transpose(s, k, g):
                turn = tile_turn(s, k)
                pe.wait_ge(rows_in[s][k], (g + 1) * (16 * turn_slots(k)))
                pe.wait_ge(turn_out[turn % 2], g * PER_BANK + (turn // 2 + 1))
                for i in range(turn_slots(k)):
                    last = nc.tensor.transpose(ps_t[turn % 2][:, i * P:(i + 1) * P], rows[:, s, 4 * k + i, :],
                                               ident[:, :])
                last.then_inc(transposed, 1)

            def layer1(c, g, parity):
                if c == 0:
                    pe.wait_ge(unit_low, (g + 1) * UNITS + 2)
                    pe.wait_ge(layer3_out, g + 1)
                else:
                    pe.wait_ge(layer1_out, g * (HID1 // P) + c)
                for part in (inter_h, inter_l):
                    for j in range(SLOT):
                        last = nc.tensor.matmul(ps_h[:, c % 2, :], w1_sb[:, j, c * P:(c + 1) * P], part[:, parity, j, :],
                                                start=(j == 0 and part is inter_h),
                                                stop=(j == SLOT - 1 and part is inter_l))
                last.then_inc(layer1_done, 1)

            def layer2(c, g):
                if c == 0:
                    pe.wait_ge(layer1_out, (g + 1) * (HID1 // P))
                else:
                    pe.wait_ge(layer2_out, g * (HID2 // P) + c)
                for j in range(HID1 // P):
                    last = nc.tensor.matmul(ps_h[:, c, :], w2_sb[:, j, c * P:(c + 1) * P], hid1[:, j, :],
                                            start=(j == 0), stop=(j == HID1 // P - 1))
                last.then_inc(layer2_done, 1)

            def layer3(g):
                pe.wait_ge(layer2_out, (g + 1) * (HID2 // P))
                for s in range(GROUP):
                    for j in range(HID2 // P):
                        last = nc.tensor.matmul(ps_h[:, 0, s:s + 1], hid2[:, j, s * P:(s + 1) * P], w3_sb[:, j:j + 1],
                                                start=(j == 0), stop=(j == HID2 // P - 1))
                last.then_inc(layer3_done, 1)

            def multiply(u, g):
                pe.wait_ge(unit_low, g * UNITS + (u + 1))
                for c in range(UNIT_SETS):
                    b = u * UNIT + c * QUADS
                    last = nc.tensor.matmul(
                        ps_g[u % 2][:, c, 0:QUADS * FEATURES].rearrange("p (b f) -> p b f", b=QUADS),
                        emb[:, b:b + QUADS, :].rearrange("p b f -> p (b f)"),
                        emb[:, b:b + QUADS, 0:FEATURES], start=True, stop=True)
                last.then_inc(unit_done, 1)

            def group(g, parity, first=False, final=False):
                for kind, *which in ORDER:
                    if kind == "tile":
                        transpose(*which, g)
                        if which == [1, 1] and not first:
                            layer1(2, g - 1, 1 - parity)
                    else:
                        for k in (which[0], which[0] + 1):
                            if first:
                                pe.wait_ge(table_split, k + 1)
                            look_up_small(k, g)
                        if not first and which[0] in (2, 4):
                            layer1(which[0] // 2 - 1, g - 1, 1 - parity)
                        if not final and which[0] == SMALL - 2:
                            pe.wait_ge(ids_row_ready, g + 2)
                            spread_ids(0, g + 1)
                if not first:
                    layer1(3, g - 1, 1 - parity)
                for i in range(2):
                    pe.wait_ge(turn_out[i], (g + 1) * PER_BANK + 1)
                for u in range(UNITS):
                    multiply(u, g)
                    if not first:
                        if u in (1, 3):
                            layer2(u // 2, g - 1)
                        if u == 5:
                            layer3(g - 1)

            pe.wait_ge(const_made, 3)
            pe.wait_ge(picks_made, 1)
            pe.wait_ge(ids_row_ready, 1)
            spread_ids(0, 0)
            pe.wait_ge(pads_zero, 1)
            group(0, 0, first=True)
            pe.wait_ge(w1_split, SLOT)
            pe.wait_ge(weights_in, 16 * 4)
            with pe.Fori(0, PAIRS) as pair:
                group(pair * 2 + 1, 1)
                group(pair * 2 + 2, 0)
            group(GROUPS - 1, 1, final=True)
            for c in range(HID1 // P):
                layer1(c, GROUPS - 1, 1)
            for c in range(HID2 // P):
                layer2(c, GROUPS - 1)
            layer3(GROUPS - 1)

        @block.scalar
        def _(act):
            def copy_small(k, g):
                turn = small_turn(k)
                act.wait_ge(onehot_used[1], g * (SMALL // 2) + (k // 2 + 2))
                nc.scalar.copy(emb[:, :, LARGE + k:LARGE + k + 2], ps_t[turn % 2][:, :].rearrange("p (f b) -> p b f", f=2)
                               ).then_inc(turn_out[turn % 2], 1)

            def copy_tile(s, k, g):
                turn, n = tile_turn(s, k), turn_slots(k)
                act.wait_ge(transposed, g * (GROUP * TURNS) + (s * TURNS + k + 1))
                nc.scalar.copy(emb[:, s * P:(s + 1) * P, 4 * k:4 * k + n],
                               ps_t[turn % 2][:, 0:n * P].rearrange("p (f b) -> p b f", f=n)
                               ).then_inc(turn_out[turn % 2], 1)

            def layer1_act(c, g):
                act.wait_ge(layer1_done, g * (HID1 // P) + (c + 1))
                nc.scalar.activation(hid1[:, c, :], ps_h[:, c % 2, :], ACT.Relu, bias=b1_sb[:, c:c + 1]
                                     ).then_inc(layer1_out, 1)

            def layer2_act(c, g):
                act.wait_ge(layer2_done, g * (HID2 // P) + (c + 1))
                nc.scalar.activation(hid2[:, c, :], ps_h[:, c, :], ACT.Relu, bias=b2_sb[:, c:c + 1]
                                     ).then_inc(layer2_out, 1)

            def layer3_act(g):
                act.wait_ge(layer3_done, g + 1)
                nc.scalar.copy(y_sb[:, bass.ds(g * GROUP, GROUP)], ps_h[:, 0, 0:GROUP]).then_inc(layer3_out, 1)

            def high_parts(u, g, parity):
                act.wait_ge(unit_done, g * UNITS + (u + 1))
                for j in range(QUADS):
                    for q in range(QUADS):
                        to, of = block_aps(u, j, q, inter_h[:, parity])
                        last = nc.scalar.copy(to, of)
                    last.then_inc(unit_high, 1)

            def group(g, parity, first=False):
                for kind, *which in ORDER:
                    if kind == "small":
                        copy_small(*which, g)
                        if not first and which[0] in (2, 4):
                            layer1_act(which[0] // 2 - 1, g - 1)
                        continue
                    copy_tile(*which, g)
                    if which == [1, 1] and not first:
                        layer1_act(2, g - 1)
                nc.scalar.copy(inter_h[CTX_AT:P, parity, SLOT - 1, :], side[CTX_AT:P, bass.ds(g * WIDE, WIDE)])
                if not first:
                    layer1_act(3, g - 1)
                for u in range(UNITS):
                    high_parts(u, g, parity)
                    if not first:
                        if u in (1, 3):
                            layer2_act(u // 2, g - 1)
                        if u == 5:
                            layer3_act(g - 1)

            act.sem_inc(turn_out[0], 1)
            act.sem_inc(turn_out[1], 1)
            act.sem_inc(layer3_out, 1)
            for n in range(SMALL):
                act.wait_ge(table_in[n], 16)
                nc.scalar.copy(table_h[0:ROWS_P, n, :, :].rearrange("p c d -> p (c d)"), raw_table[0:ROWS_P, n, :]
                               ).then_inc(table_high, 1)
            for j in range(SLOT):
                act.wait_ge(w1_in[j], 32)
                nc.scalar.copy(w1_sb[:, j, :], raw_w1[j % len(raw_w1)][:, 0, :])
                if j:
                    act.wait_ge(w1_split, j)
                nc.scalar.copy(low_h, raw_w1[j % len(raw_w1)][:, 1, :]).then_inc(w1_high, 1)
            act.wait_ge(table_split, SMALL)
            act.wait_ge(ctx_in, 32)
            act.wait_ge(weights_in, 16 * 4)
            group(0, 0, first=True)
            with act.Fori(0, PAIRS) as pair:
                group(pair * 2 + 1, 1)
                group(pair * 2 + 2, 0)
            group(GROUPS - 1, 1)
            for c in range(HID1 // P):
                layer1_act(c, GROUPS - 1)
            for c in range(HID2 // P):
                layer2_act(c, GROUPS - 1)
            layer3_act(GROUPS - 1)

        @block.vector
        def _(dve):
            def cast_ids(g):
                nc.vector.tensor_copy(ids_row[:, :], side[0:SMALL, bass.ds(g * WIDE, WIDE)].bitcast(int32)
                                      ).then_inc(ids_row_ready, 1)

            def compare(k, g):
                dve.wait_ge(ids_spread, g * (SMALL // 2) + (k // 2 + 1))
                dve.wait_ge(onehot_used[k % 2], g * (SMALL // 2) + (k // 2 + 1))
                nc.vector.tensor_tensor(
                    onehot[0:ROWS_P, k % 2, :, :],
                    ps_i[0:ROWS_P, k % 2, :].unsqueeze(1).to_broadcast([ROWS_P, CHUNKS, WIDE]),
                    row_no[0:ROWS_P, :].unsqueeze(2).to_broadcast([ROWS_P, CHUNKS, WIDE]),
                    ALU.is_equal).then_inc(onehot_ready[k % 2], 1)

            def split_table(n):
                dve.wait_ge(table_high, n + 1)
                high = table_h[0:ROWS_P, n, :, :].rearrange("p c d -> p (c d)").bitcast(fp32)
                nc.vector.tensor_tensor(table_l[0:ROWS_P, n, :, :].rearrange("p c d -> p (c d)"),
                                        raw_table[0:ROWS_P, n, :], high, ALU.subtract).then_inc(table_split, 1)

            def split_weights(j):
                dve.wait_ge(w1_high, j + 1)
                nc.vector.tensor_tensor(low_raw, raw_w1[j % len(raw_w1)][:, 1, :], low_h.bitcast(fp32), ALU.subtract
                                        ).then_inc(low_made, 1)
                dve.wait_ge(low_made, j + 1)
                nc.vector.tensor_tensor(w1_sb[:, j, :], w1_sb[:, j, :].bitcast(fp32), low_raw, ALU.add
                                        ).then_inc(w1_split, 1)

            def low_parts(g, parity):
                for u in range(UNITS):
                    for j in range(QUADS):
                        dve.wait_ge(unit_high, g * (UNITS * QUADS) + (u * QUADS + j + 1))
                        if u == 0 and j == 0:
                            nc.vector.tensor_tensor(
                                inter_l[CTX_AT:P, parity, SLOT - 1, :], side[CTX_AT:P, bass.ds(g * WIDE, WIDE)],
                                inter_h[CTX_AT:P, parity, SLOT - 1, :].bitcast(fp32), ALU.subtract)
                        for q in range(QUADS):
                            to, of = block_aps(u, j, q, inter_l[:, parity])
                            high, _ = block_aps(u, j, q, inter_h[:, parity])
                            last = nc.vector.tensor_tensor(to, of, high.bitcast(fp32), ALU.subtract)
                    last.then_inc(unit_low, 1)

            dve.sem_inc(onehot_used[0], 1)
            dve.sem_inc(onehot_used[1], 1)
            dve.sem_inc(unit_low, 2)
            dve.wait_ge(const_made, 3)
            nc.vector.tensor_copy(picks[:, :, :], hid1[0:SMALL, :, :].rearrange("p c d -> p (c d)")
                                  .rearrange("p (k d) -> p k d", k=SMALL)).then_inc(picks_made, 1)
            nc.vector.tensor_copy(row_no[:, :], row_int[:, :]).then_inc(row_no_made, 1)
            dve.wait_ge(ids_small_in, 16)
            cast_ids(0)
            dve.wait_ge(row_no_made, 1)
            for k in range(2):
                compare(k, 0)
            for n in range(SMALL):
                split_table(n)
            dve.wait_ge(table_split, SMALL)
            nc.vector.memset(emb[:, :, FEATURES:QUAD], 0.0).then_inc(pads_zero, 1)
            for j in range(SLOT):
                split_weights(j)
            for k in range(2, SMALL):
                compare(k, 0)
            cast_ids(1)
            for k in range(2):
                compare(k, 1)
            dve.wait_ge(ctx_in, 32)
            low_parts(0, 0)
            with dve.Fori(0, PAIRS) as pair:
                for now, parity in ((pair * 2 + 1, 1), (pair * 2 + 2, 0)):
                    for k in range(2, SMALL):
                        compare(k, now)
                    cast_ids(now + 1)
                    for k in range(2):
                        compare(k, now + 1)
                    low_parts(now, parity)
            for k in range(2, SMALL):
                compare(k, GROUPS - 1)
            low_parts(GROUPS - 1, 1)


def spread_rows(w_top1, order):
    upper = np.zeros((P, SLOT, HID1), w_top1.dtype)
    lower = np.zeros((P, SLOT, HID1), w_top1.dtype)
    place = np.argsort(order)
    first, second = (place[i] for i in np.triu_indices(FEATURES, k=1))
    n, m = np.minimum(first, second), np.maximum(first, second)
    upper[QUAD * (m // SLOT) + n, m % SLOT] = w_top1[:len(first)]
    lower[QUAD * (n // SLOT) + m, n % SLOT] = w_top1[:len(first)]
    upper[CTX_AT:CTX_AT + CTX, SLOT - 1] = w_top1[len(first):]
    lower[CTX_AT + CTX:P, SLOT - 1] = w_top1[len(first):]
    return upper, lower


def kernel(**inputs):
    import concourse.bacc as bacc
    from concourse.bass_utils import run_bass_kernel_spmd

    nc = bacc.Bacc("TRN2", target_bir_lowering=False, num_devices=1)
    arrays = {}

    def dram(name, a):
        arrays[name] = a = np.ascontiguousarray(a)
        return nc.dram_tensor(name, a.shape, mybir.dt.from_np(a.dtype), kind="ExternalInput").ap()

    x = {name: np.asarray(a) for name, a in inputs.items()}
    tables = [x[f"tbl_{f}"] for f in range(FEATURES)]
    small = [f for f in range(FEATURES) if len(tables[f]) == SMALL_ROWS]
    large = [f for f in range(FEATURES) if len(tables[f]) != SMALL_ROWS]
    upper, lower = spread_rows(x["W_top1"], large + small)
    out = nc.dram_tensor("y", (BATCH, 1), mybir.dt.float32, kind="ExternalOutput").ap()
    by_tile = x["ids"].reshape(P, TILES, FEATURES)
    tower(
        nc,
        dram("ids", by_tile[:, :, large].reshape(P, TILES * LARGE)),
        dram("ids_small", by_tile[:, :, small].transpose(2, 1, 0).reshape(SMALL, BATCH)),
        [dram(f"tbl_{f}", tables[f]) for f in large],
        [dram(f"tbl_{f}", tables[f]) for f in small],
        dram("dense_ctx", x["dense_ctx"].reshape(P, TILES, CTX).transpose(2, 1, 0).reshape(CTX, BATCH)),
        dram("w1_upper", upper),
        dram("w1_lower", lower),
        dram("b1", x["b_top1"].reshape(HID1 // P, P).T),
        dram("w2", x["W_top2"].reshape(HID1 // P, P, HID2).transpose(1, 0, 2)),
        dram("b2", x["b_top2"].reshape(HID2 // P, P).T),
        dram("w3", x["W_top3"].reshape(HID2 // P, P).T),
        out.rearrange("(p t) o -> p (t o)", p=P),
    )
    results = run_bass_kernel_spmd(nc, [arrays], core_ids=[0]).results[0]
    return results["y"]
```

```python
from contextlib import ExitStack

import numpy as np

import concourse.bass as bass
from concourse import mybir

P = 128
FEATURES = 27
DIM = 128
BATCH = 2048
CTX = 16
HID1, HID2 = 512, 256
TILES = BATCH // P
GROUP = 2
GROUPS = TILES // GROUP
WIDE = GROUP * P
QUAD = 32
QUADS = P // QUAD
P_GRAM = (QUADS - 1) * QUAD + FEATURES
SLOT = 7
UNIT_SETS = 8
UNIT = UNIT_SETS * QUADS
UNITS = WIDE // UNIT
TILE_UNITS = UNITS // GROUP
SHARE_UNITS = 2
SHARES = UNITS // SHARE_UNITS
SMALL_ROWS = 1000
CHUNKS = 8
ROWS_P = SMALL_ROWS // CHUNKS
SMALL = 8
RAW = 5
LARGE = FEATURES - SMALL
TURNS = (LARGE + 3) // 4
SMALL_TURNS = (SMALL + 1) // 2
GROUP_TURNS = SMALL_TURNS + GROUP * TURNS
PER_BANK = GROUP_TURNS // 2
ONEHOTS = [(SMALL + 1) // 2, SMALL // 2]
CTX_AT = P - QUAD


def turn_slots(k):
    return min(4, LARGE - 4 * k)


STEPS = [("tile", 0, 0), ("layer1", 0), ("tile", 0, 1), ("small", 4), ("tile", 0, 2), ("layer1", 1),
         ("tile", 0, 3), ("small", 6), ("tile", 0, 4), ("layer1", 2), ("unit", 0), ("layer1", 3),
         ("tile", 1, 0), ("unit", 1), ("layer2", 0), ("tile", 1, 1), ("unit", 2), ("tile", 1, 2),
         ("tile", 1, 3), ("unit", 3), ("tile", 1, 4), ("next small", 0), ("unit", 4), ("unit", 5),
         ("unit", 6), ("unit", 7), ("layer2", 1), ("next small", 2)]
ORDER = [("small", 0), ("small", 2)] + [step for step in STEPS if step[0] in ("small", "tile")]
HIGH_AFTER_TURN = {2: [0], 3: [1], 4: [2], 5: [3], 6: [4], GROUP_TURNS - 1: [5, 6]}
SPLIT_AFTER_UNIT = {0: [0, 1], 1: [2, 3], 2: [4], 7: [5, 6]}
TABLES_FIRST = 5


def turn_tables(k):
    return range(k, min(k + 2, SMALL))


def small_turn(k):
    return ORDER.index(("small", k - k % 2))


def tile_turn(s, k):
    return ORDER.index(("tile", s, k))


def tower(nc, ids, ids_small, large_tables, small_tables, ctx_t, w1, w1_sides, b1, w2, b2, w3, out):
    fp32, fp32r, int32 = mybir.dt.float32, mybir.dt.float32r, mybir.dt.int32
    ACT = mybir.ActivationFunctionType
    ALU = mybir.AluOpType
    with ExitStack() as stack:
        def sb(name, shape, dt=fp32):
            return stack.enter_context(nc.sbuf_tensor(name, shape, dt))

        def sem(name):
            return stack.enter_context(nc.semaphore(name))

        ids_sb = sb("ids_sb", [P, TILES * LARGE], int32)
        ids_now = sb("ids_now", [P, GROUP, LARGE], int32)
        rows = sb("rows", [P, GROUP, LARGE, DIM])
        ctx_sb = sb("ctx_sb", [P, BATCH])
        ids_wide = sb("ids_wide", [P, SMALL, WIDE], int32)
        raw = sb("raw", [P, RAW, HID1])
        sides = sb("sides", [P, 2, SLOT])
        row_int = sb("row_int", [P, CHUNKS], int32)
        table_h = sb("table_h", [P, SMALL, CHUNKS, DIM], fp32r)
        table_l = sb("table_l", [P, SMALL, CHUNKS, DIM], fp32r)
        onehot = sb("onehot", [P, 2, CHUNKS, WIDE], fp32r)
        emb = sb("emb", [P, WIDE, QUAD])
        inter = sb("inter", [P, SLOT, WIDE])
        inter_h = sb("inter_h", [P, SLOT, WIDE], fp32r)
        inter_l = sb("inter_l", [P, SLOT, WIDE], fp32r)
        hid1 = sb("hid1", [P, HID1 // P, WIDE])
        hid2 = sb("hid2", [P, GROUP, HID2])
        raw_table = emb[:, :, :].rearrange("p b f -> p (b f)").rearrange("p (n c) -> p n c", c=CHUNKS * DIM)
        w2_sb = sb("w2_sb", [P, HID1 // P, HID2])
        w1_sb = sb("w1_sb", [P, SLOT, HID1], fp32r)
        w3_sb = sb("w3_sb", [P, HID2])
        b1_sb = sb("b1_sb", [P, HID1 // P])
        b2_sb = sb("b2_sb", [P, HID2])
        ident = sb("ident", [P, P])
        zero = sb("zero", [P, 1])
        y_sb = sb("y_sb", [P, TILES])

        ps_t = [stack.enter_context(nc.psum_tensor(f"ps_t{i}", [P, 4 * P], fp32)) for i in range(2)]
        ps_g = [stack.enter_context(nc.psum_tensor(f"ps_g{i}", [P, UNIT_SETS, P], fp32)) for i in range(2)]
        ps_h = [stack.enter_context(nc.psum_tensor(f"ps_h{i}", [P, 2 * WIDE], fp32)) for i in range(2)]

        ids_in = sem("ids_in")
        ids_staged = sem("ids_staged")
        pool_passed = sem("pool_passed")
        ctx_sides_in = sem("ctx_sides_in")
        weights_in = sem("weights_in")
        table_in = [sem(f"table_in_{n}") for n in range(SMALL)]
        table_high = sem("table_high")
        table_split = sem("table_split")
        w1_in = [sem(f"w1_in_{j}") for j in range(SLOT)]
        w1_high = sem("w1_high")
        w1_split = sem("w1_split")
        const_zero = sem("const_zero")
        const_made = sem("const_made")
        pads_zero = sem("pads_zero")
        ids_wide_in = [sem(f"ids_wide_in_{i}") for i in range(SMALL_TURNS)]
        onehot_ready = [sem(f"onehot_ready_{i}") for i in range(2)]
        onehot_used = [sem(f"onehot_used_{i}") for i in range(2)]
        rows_in = [[sem(f"rows_in_{s}_{k}") for k in range(TURNS)] for s in range(GROUP)]
        transposed = sem("transposed")
        turn_out = [sem(f"turn_out_{i}") for i in range(2)]
        unit_done = sem("unit_done")
        unit_out_act = sem("unit_out_act")
        unit_out_dve = sem("unit_out_dve")
        inter_high = sem("inter_high")
        inter_low = sem("inter_low")
        layer1_done = sem("layer1_done")
        layer1_out = sem("layer1_out")
        layer2_done = sem("layer2_done")
        layer2_out = sem("layer2_out")
        layer3_out = sem("layer3_out")
        out_stored = sem("out_stored")

        def copy_blocks(copy, u, which, done):
            for j in which:
                for q in range(QUADS):
                    n = min(SLOT, FEATURES - q * SLOT)
                    to = inter[QUAD * q:QUAD * q + FEATURES, 0:n, u * UNIT:(u + 1) * UNIT]
                    last = copy(to.rearrange("p m (c b) -> p b c m", b=QUADS)[:, j],
                                ps_g[u % 2][QUAD * j:QUAD * j + FEATURES, :,
                                            j * FEATURES + q * SLOT:j * FEATURES + q * SLOT + n])
            last.then_inc(done, 1)

        block = stack.enter_context(nc.Block())

        @block.sync
        def _(sp):
            def load_ids(k, g):
                tables = turn_tables(k)
                sp.dma_start(ids_wide[0:ROWS_P, k:tables[-1] + 1, :],
                             ids_small[k:tables[-1] + 1, bass.ds(g * WIDE, WIDE)].unsqueeze(0)
                             .to_broadcast([ROWS_P, len(tables), WIDE])).then_inc(ids_wide_in[k // 2], 16)

            def load_next_ids(g):
                for k in range(0, SMALL, 2):
                    end = turn_tables(k)[-1]
                    sp.wait_ge(onehot_ready[end % 2], (g - 1) * ONEHOTS[end % 2] + (k // 2 + 1))
                    load_ids(k, g)

            def load_w1(j):
                sp.dma_start(raw[:, j % RAW, :], w1[:, j, :]).then_inc(w1_in[j], 16)

            load_ids(0, 0)
            for n in range(SMALL):
                sp.dma_start(raw_table[0:ROWS_P, n, :], small_tables[n].rearrange("(p c) d -> p (c d)", c=CHUNKS)
                             ).then_inc(table_in[n], 16)
            for k in range(2, SMALL, 2):
                load_ids(k, 0)
            sp.dma_start(sides[:, :, :], w1_sides).then_inc(ctx_sides_in, 16)
            for copy in range(2):
                sp.dma_start(ctx_sb[CTX_AT + copy * CTX:CTX_AT + (copy + 1) * CTX, :], ctx_t
                             ).then_inc(ctx_sides_in, 16)
            sp.dma_start(w2_sb[:, :, :], w2).then_inc(weights_in, 16)
            sp.dma_start(b1_sb[:, :], b1).then_inc(weights_in, 16)
            sp.dma_start(b2_sb[:, :], b2.to_broadcast([P, HID2])).then_inc(weights_in, 16)
            sp.dma_start(w3_sb[:, :], w3.to_broadcast([P, HID2])).then_inc(weights_in, 16)
            for j in range(RAW):
                load_w1(j)
            load_next_ids(1)
            for j in range(RAW, SLOT):
                sp.wait_ge(w1_split, j + 1 - RAW)
                load_w1(j)
            with sp.Fori(2, GROUPS) as g:
                load_next_ids(g)
            sp.wait_ge(layer3_out, TILES)
            sp.dma_start(out, y_sb[:, :]).then_inc(out_stored, 16)
            sp.wait_ge(out_stored, 16)

        @block.gpsimd
        def _(pool):
            def gather_tile(indices, s):
                for i in range(LARGE):
                    nc.gpsimd.indirect_dma_start(
                        rows[:, s, i, :], None, large_tables[i],
                        bass.IndirectOffsetOnAxis(ap=indices[:, i:i + 1], axis=0),
                    ).then_inc(rows_in[s][i // 4], 16)

            nc.gpsimd.memset(ident[:, :], 0.0).then_inc(const_zero, 1)
            nc.gpsimd.memset(zero[:, :], 0.0).then_inc(const_made, 1)
            pool.wait_ge(const_zero, 1)
            nc.gpsimd.affine_select(out=ident[:, :], in_=ident[:, :], compare_op=ALU.not_equal, fill=1.0,
                                    base=0, pattern=[[-1, P]], channel_multiplier=1).then_inc(const_made, 1)
            nc.gpsimd.iota(row_int[:, :], pattern=[[1, CHUNKS]], base=0,
                           channel_multiplier=CHUNKS).then_inc(const_made, 1)
            pool.wait_ge(ids_in, 16)
            for s in range(GROUP):
                gather_tile(ids_sb[:, s * LARGE:(s + 1) * LARGE], s)
            with pool.Fori(1, GROUPS) as g:
                for s in range(GROUP):
                    pool.wait_ge(ids_staged, (g - 1) * GROUP + (s + 1))
                    pool.sem_inc(pool_passed, 1)
                    gather_tile(ids_now[:, s, :], s)

        @block.tensor
        def _(pe):
            def look_up_small(k, g):
                turn = small_turn(k)
                pe.wait_ge(onehot_ready[k % 2], g * ONEHOTS[k % 2] + (k // 2 + 1))
                if k % 2 == 0:
                    pe.wait_ge(turn_out[turn % 2], g * PER_BANK + (turn // 2 + 1))
                to = ps_t[turn % 2][:, (k % 2) * WIDE:(k % 2 + 1) * WIDE]
                for c in range(CHUNKS):
                    for part in (table_h, table_l):
                        last = nc.tensor.matmul(to, part[0:ROWS_P, k, c, :], onehot[0:ROWS_P, k % 2, c, :],
                                                start=(c == 0 and part is table_h),
                                                stop=(c == CHUNKS - 1 and part is table_l))
                last.then_inc(onehot_used[k % 2], 1)

            def transpose(s, k, g):
                turn = tile_turn(s, k)
                pe.wait_ge(rows_in[s][k], (g + 1) * (16 * turn_slots(k)))
                pe.wait_ge(turn_out[turn % 2], g * PER_BANK + (turn // 2 + 1))
                for i in range(turn_slots(k)):
                    last = nc.tensor.transpose(ps_t[turn % 2][:, i * P:(i + 1) * P], rows[:, s, 4 * k + i, :],
                                               ident[:, :])
                last.then_inc(transposed, 1)

            def layer1(c, g):
                if c == 0:
                    pe.wait_ge(inter_high, (g + 1) * SHARES)
                    pe.wait_ge(layer2_out, g * GROUP + 1)
                elif c >= 2:
                    pe.wait_ge(layer1_out, g * (HID1 // P) + (c - 1))
                for part in (inter_h, inter_l):
                    if part is inter_l and c == 0:
                        pe.wait_ge(inter_low, (g + 1) * SHARES)
                    for j in range(SLOT):
                        last = nc.tensor.matmul(ps_h[c % 2][:, 0:WIDE], w1_sb[:, j, c * P:(c + 1) * P], part[:, j, :],
                                                start=(j == 0 and part is inter_h),
                                                stop=(j == SLOT - 1 and part is inter_l))
                last.then_inc(layer1_done, 1)

            def layer2(s, g):
                if s == 0:
                    pe.wait_ge(layer1_out, g * (HID1 // P) + (HID1 // P - 1))
                for j in range(HID1 // P):
                    if j == HID1 // P - 1 and s == 0:
                        pe.wait_ge(layer1_out, (g + 1) * (HID1 // P))
                    last = nc.tensor.matmul(ps_h[s][:, 0:HID2], hid1[:, j, s * P:(s + 1) * P], w2_sb[:, j, :],
                                            start=(j == 0), stop=(j == HID1 // P - 1))
                last.then_inc(layer2_done, 1)

            def multiply(u, g):
                pe.wait_ge(unit_out_act, g * UNITS + (u + 1))
                pe.wait_ge(unit_out_dve, g * UNITS + (u + 1))
                for c in range(UNIT_SETS):
                    b = u * UNIT + c * QUADS
                    last = nc.tensor.matmul(
                        ps_g[u % 2][0:P_GRAM, c, 0:QUADS * FEATURES].rearrange("p (b f) -> p b f", b=QUADS),
                        emb[:, b:b + QUADS, :].rearrange("p b f -> p (b f)")[:, 0:P_GRAM],
                        emb[:, b:b + QUADS, 0:FEATURES], start=True, stop=True)
                last.then_inc(unit_done, 1)

            def embeddings_whole(turns, g):
                pe.wait_ge(turn_out[0], g * PER_BANK + ((turns + 1) // 2 + 1))
                pe.wait_ge(turn_out[1], g * PER_BANK + (turns // 2 + 1))

            def look_up_pair(k, g):
                for i in turn_tables(k):
                    look_up_small(i, g)

            def group(g, first=False, final=False):
                for kind, *which in STEPS:
                    if kind == "tile":
                        transpose(*which, g)
                    elif kind == "small":
                        if first:
                            pe.wait_ge(table_split, turn_tables(*which)[-1] + 1)
                        look_up_pair(*which, g)
                    elif kind == "unit":
                        if which[0] == 0:
                            embeddings_whole(tile_turn(1, 0), g)
                        if which[0] == TILE_UNITS:
                            embeddings_whole(GROUP_TURNS, g)
                        multiply(*which, g)
                    elif kind == "next small" and not final:
                        look_up_pair(*which, g + 1)
                    elif kind == "layer1" and not first:
                        layer1(*which, g - 1)
                    elif kind == "layer2" and not first:
                        layer2(*which, g - 1)

            pe.wait_ge(const_made, 3)
            for k in range(4):
                pe.wait_ge(table_split, k + 1)
                look_up_small(k, 0)
            pe.wait_ge(pads_zero, 1)
            group(0, first=True)
            pe.wait_ge(w1_split, SLOT)
            pe.wait_ge(weights_in, 16 * 4)
            with pe.Fori(1, GROUPS - 1) as g:
                group(g)
            group(GROUPS - 1, final=True)
            for c in range(HID1 // P):
                layer1(c, GROUPS - 1)
            for s in range(GROUP):
                layer2(s, GROUPS - 1)

        @block.scalar
        def _(act):
            def copy_small(k, g):
                turn, tables = small_turn(k), turn_tables(k)
                end, n = tables[-1], len(tables)
                act.wait_ge(onehot_used[end % 2], g * ONEHOTS[end % 2] + (k // 2 + 2))
                nc.scalar.copy(emb[:, :, LARGE + k:LARGE + k + n],
                               ps_t[turn % 2][:, 0:n * WIDE].rearrange("p (f b) -> p b f", f=n)
                               ).then_inc(turn_out[turn % 2], 1)

            def copy_tile(s, k, g, final):
                turn, n = tile_turn(s, k), turn_slots(k)
                act.wait_ge(transposed, g * (GROUP * TURNS) + (s * TURNS + k + 1))
                nc.scalar.copy(emb[:, s * P:(s + 1) * P, 4 * k:4 * k + n],
                               ps_t[turn % 2][:, 0:n * P].rearrange("p (f b) -> p b f", f=n)
                               ).then_inc(turn_out[turn % 2], 1)
                if k == TURNS - 1 and not final:
                    nc.scalar.copy(ids_now[:, s, :], ids_sb[:, bass.ds((g + 1) * (GROUP * LARGE) + s * LARGE, LARGE)]
                                   ).then_inc(ids_staged, 1)

            def layer1_act(c, g):
                act.wait_ge(layer1_done, g * (HID1 // P) + (c + 1))
                nc.scalar.activation(hid1[:, c, :], ps_h[c % 2][:, 0:WIDE], ACT.Relu, bias=b1_sb[:, c:c + 1]
                                     ).then_inc(layer1_out, 1)

            def split_high(s, g):
                act.wait_ge(unit_out_act, g * UNITS + (s + 1) * SHARE_UNITS + 2)
                act.wait_ge(unit_out_dve, g * UNITS + (s + 1) * SHARE_UNITS + 2)
                share = slice(s * SHARE_UNITS * UNIT, (s + 1) * SHARE_UNITS * UNIT)
                nc.scalar.copy(inter_h[:, :, share], inter[:, :, share]).then_inc(inter_high, 1)

            def high_weights(j):
                act.wait_ge(w1_in[j], 16)
                nc.scalar.activation(w1_sb[:, j, :], raw[:, j % RAW, :], ACT.Copy, scale=sides[:, 0, j:j + 1]
                                     ).then_inc(w1_high, 1)

            def group(g, first=False, final=False):
                for kind, *which in STEPS:
                    if kind == "tile":
                        copy_tile(*which, g, final)
                    elif kind == "small":
                        copy_small(*which, g)
                    elif kind == "unit":
                        u = which[0]
                        act.wait_ge(unit_done, g * UNITS + (u + 1))
                        if u == 0:
                            nc.scalar.copy(inter[CTX_AT:P, SLOT - 1, :], ctx_sb[CTX_AT:P, bass.ds(g * WIDE, WIDE)])
                        copy_blocks(nc.scalar.copy, u, (2, 3), unit_out_act)
                        if u > 0 and u % SHARE_UNITS == 0:
                            split_high(u // SHARE_UNITS - 1, g)
                        if u == UNITS - 1:
                            if not final:
                                copy_small(0, g + 1)
                            split_high(SHARES - 1, g)
                    elif kind == "next small" and which[0] == 2 and not final:
                        copy_small(2, g + 1)
                    elif kind == "layer1" and not first:
                        layer1_act(*which, g - 1)
                    if first and kind in ("tile", "small"):
                        for j in HIGH_AFTER_TURN.get(ORDER.index((kind, *which)), []):
                            high_weights(j)

            act.dma_start(ids_sb[:, :], ids).then_inc(ids_in, 16)
            act.sem_inc(unit_out_act, 2)
            act.sem_inc(turn_out[0], 1)
            act.sem_inc(turn_out[1], 1)
            act.sem_inc(layer2_out, 1)
            act.wait_ge(const_made, 3)
            nc.scalar.copy(inter[:, :, :], zero[:, :].unsqueeze(2).to_broadcast([P, SLOT, WIDE]))
            for n in range(SMALL):
                act.wait_ge(table_in[n], 16)
                nc.scalar.copy(table_h[0:ROWS_P, n, :, :].rearrange("p c d -> p (c d)"), raw_table[0:ROWS_P, n, :]
                               ).then_inc(table_high, 1)
            act.wait_ge(ids_in, 16)
            act.wait_ge(ctx_sides_in, 16 * 3)
            act.wait_ge(table_split, SMALL)
            nc.scalar.copy(emb[:, :, FEATURES:QUAD], zero[:, :].unsqueeze(2).to_broadcast([P, WIDE, QUAD - FEATURES])
                           ).then_inc(pads_zero, 1)
            for k in (0, 2):
                copy_small(k, 0)
            group(0, first=True)
            act.wait_ge(weights_in, 16 * 4)
            with act.Fori(1, GROUPS - 1) as g:
                group(g)
            group(GROUPS - 1, final=True)
            for c in range(HID1 // P):
                layer1_act(c, GROUPS - 1)

        @block.vector
        def _(dve):
            def compare(k, g):
                dve.wait_ge(ids_wide_in[k // 2], 16 * (g + 1))
                dve.wait_ge(onehot_used[k % 2], g * ONEHOTS[k % 2] + (k // 2 + 1))
                nc.vector.tensor_tensor(
                    onehot[0:ROWS_P, k % 2, :, :],
                    ids_wide[0:ROWS_P, k, :].unsqueeze(1).to_broadcast([ROWS_P, CHUNKS, WIDE]),
                    row_int[0:ROWS_P, :].unsqueeze(2).to_broadcast([ROWS_P, CHUNKS, WIDE]),
                    ALU.is_equal).then_inc(onehot_ready[k % 2], 1)

            def split_table(n):
                dve.wait_ge(table_high, n + 1)
                high = table_h[0:ROWS_P, n, :, :].rearrange("p c d -> p (c d)").bitcast(fp32)
                nc.vector.tensor_tensor(table_l[0:ROWS_P, n, :, :].rearrange("p c d -> p (c d)"),
                                        raw_table[0:ROWS_P, n, :], high, ALU.subtract).then_inc(table_split, 1)

            def split_weights(j):
                dve.wait_ge(w1_high, j + 1)
                nc.vector.scalar_tensor_tensor(w1_sb[:, j, :], raw[:, j % RAW, :], sides[:, 1, j:j + 1],
                                               w1_sb[:, j, :].bitcast(fp32), ALU.mult, ALU.subtract
                                               ).then_inc(w1_split, 1)

            def split_low(s, g):
                dve.wait_ge(inter_high, g * SHARES + (s + 1))
                share = slice(s * SHARE_UNITS * UNIT, (s + 1) * SHARE_UNITS * UNIT)
                nc.vector.tensor_tensor(inter_l[:, :, share], inter[:, :, share], inter_h[:, :, share].bitcast(fp32),
                                        ALU.subtract).then_inc(inter_low, 1)

            def score(s, g):
                dve.wait_ge(layer2_done, g * GROUP + (s + 1))
                nc.vector.tensor_tensor(hid2[:, s, :], ps_h[s][:, 0:HID2], b2_sb[:, :], ALU.add).then_inc(layer2_out, 1)
                dve.wait_ge(layer2_out, g * GROUP + (s + 2))
                nc.vector.scalar_tensor_tensor(hid2[:, s, :], hid2[:, s, :], 0.0, w3_sb[:, :], ALU.max, ALU.mult,
                                               accum_out=y_sb[:, bass.ds(g * GROUP + s, 1)]).then_inc(layer3_out, 1)

            def group(g, first=False, final=False):
                for k in range(4, SMALL):
                    compare(k, g)
                if not final:
                    for k in range(2):
                        compare(k, g + 1)
                for u in range(UNITS):
                    if u == TILE_UNITS and not final:
                        compare(2, g + 1)
                    dve.wait_ge(unit_done, g * UNITS + (u + 1))
                    copy_blocks(nc.vector.tensor_copy, u, (0, 1), unit_out_dve)
                    if first:
                        for j in SPLIT_AFTER_UNIT.get(u, []):
                            split_weights(j)
                    if u > 0 and u % SHARE_UNITS == 0:
                        split_low(u // SHARE_UNITS - 1, g)
                    if u == 2 and not first:
                        score(0, g - 1)
                    if u == TILE_UNITS + 1 and not final:
                        compare(3, g + 1)
                if not first:
                    score(1, g - 1)
                split_low(SHARES - 1, g)

            dve.sem_inc(onehot_used[0], 1)
            dve.sem_inc(onehot_used[1], 1)
            dve.sem_inc(unit_out_dve, 2)
            dve.wait_ge(const_made, 3)
            for k in range(2):
                compare(k, 0)
            for n in range(TABLES_FIRST):
                split_table(n)
            for k in range(2, 4):
                compare(k, 0)
            for n in range(TABLES_FIRST, SMALL):
                split_table(n)
            group(0, first=True)
            dve.wait_ge(weights_in, 16 * 4)
            with dve.Fori(1, GROUPS - 1) as g:
                group(g)
            group(GROUPS - 1, final=True)
            for s in range(GROUP):
                score(s, GROUPS - 1)


def spread_rows(w_top1, order):
    w = np.zeros((P, SLOT, HID1), w_top1.dtype)
    place = np.argsort(order)
    n, m = (place[i] for i in np.triu_indices(FEATURES, k=1))
    w[QUAD * (m // SLOT) + n, m % SLOT] = w_top1[:len(n)]
    w[QUAD * (n // SLOT) + m, n % SLOT] = w_top1[:len(n)]
    w[CTX_AT:CTX_AT + CTX, SLOT - 1] = w_top1[len(n):]
    w[CTX_AT + CTX:P, SLOT - 1] = w_top1[len(n):]
    return w


def low_places():
    low = np.zeros((P, SLOT), np.float32)
    for q in range(QUADS):
        for j in range(SLOT):
            low[QUAD * q + min(SLOT * q + j, QUAD):QUAD * (q + 1), j] = 1.0
    low[CTX_AT:P, SLOT - 1] = np.arange(QUAD) >= CTX
    return low


def kernel(**inputs):
    import concourse.bacc as bacc
    from concourse.bass_utils import run_bass_kernel_spmd

    nc = bacc.Bacc("TRN2", target_bir_lowering=False, num_devices=1)
    arrays = {}

    def dram(name, a):
        arrays[name] = a = np.ascontiguousarray(a)
        return nc.dram_tensor(name, a.shape, mybir.dt.from_np(a.dtype), kind="ExternalInput").ap()

    x = {name: np.asarray(a) for name, a in inputs.items()}
    tables = [x[f"tbl_{f}"] for f in range(FEATURES)]
    small = [f for f in range(FEATURES) if len(tables[f]) == SMALL_ROWS][:SMALL]
    large = [f for f in range(FEATURES) if f not in small]
    low = low_places()
    out = nc.dram_tensor("y", (BATCH, 1), mybir.dt.float32, kind="ExternalOutput").ap()
    by_tile = x["ids"].reshape(P, TILES, FEATURES)
    tower(
        nc,
        dram("ids", by_tile[:, :, large].reshape(P, TILES * LARGE)),
        dram("ids_small", by_tile[:, :, small].transpose(2, 1, 0).reshape(SMALL, BATCH)),
        [dram(f"tbl_{f}", tables[f]) for f in large],
        [dram(f"tbl_{f}", tables[f]) for f in small],
        dram("dense_ctx", x["dense_ctx"].reshape(P, TILES, CTX).transpose(2, 1, 0).reshape(CTX, BATCH)),
        dram("w1", spread_rows(x["W_top1"], large + small)),
        dram("w1_sides", np.stack([2 * low - 1, low], axis=1)),
        dram("b1", x["b_top1"].reshape(HID1 // P, P).T),
        dram("w2", x["W_top2"].reshape(HID1 // P, P, HID2).transpose(1, 0, 2)),
        dram("b2", x["b_top2"].reshape(1, HID2)),
        dram("w3", x["W_top3"].reshape(1, HID2)),
        out.rearrange("(p t) o -> p (t o)", p=P),
    )
    results = run_bass_kernel_spmd(nc, [arrays], core_ids=[0]).results[0]
    return results["y"]
```
